# Optimizing a Trainium2 kernel written in Bass

```python
import numpy as np
import jax
import jax.numpy as jnp

def _softmax(x, axis=-1):
    return jax.nn.softmax(x, axis=axis)

def _gelu(x):
    return jax.nn.gelu(x, approximate=True)

def _silu(x):
    return jax.nn.silu(x)

def _sigmoid(x):
    return jax.nn.sigmoid(x)

def _layernorm(x, axis=-1, eps=1e-05):
    m = jnp.mean(x, axis=axis, keepdims=True)
    v = jnp.var(x, axis=axis, keepdims=True)
    return (x - m) / jnp.sqrt(v + eps)

def _scatter_add(tgt, idx, src, axis=0):
    return tgt.at[idx].add(src)

def _segment_sum(src, seg, n):
    return jax.ops.segment_sum(src, seg, n)
kernel_name = 'mk_gnn_resnorm_d2_gnn_r64_3d7cb6'

def setup_inputs(seed: int=0):
    np.random.seed(seed)
    _w = jnp.asarray

    def _rec_inputs():
        import jax
        import jax.numpy as jnp
        _gk = jax.random.key(seed)
        x = -0.0003713 + 1 * jax.random.normal(jax.random.fold_in(_gk, 1), (50000, 256), jnp.float32)
        src = jax.random.randint(jax.random.fold_in(_gk, 2), (12500,), 0, 50000, jnp.int32)
        dst = jnp.minimum((50000 * jax.random.uniform(jax.random.fold_in(_gk, 3), (12500,)) ** 2.0).astype(jnp.int32), 49999)
        _o = jnp.argsort(dst, stable=True)
        src = src[_o]
        dst = dst[_o]
        edge_attr_128 = -5.16925e-05 + 1.00005 * jax.random.normal(jax.random.fold_in(_gk, 11), (12500, 128), jnp.float32)
        return (x, src, dst, edge_attr_128)
    x, src, dst, edge_attr_128 = _rec_inputs()

    def _L0_gnn_setup():
        import jax, jax.numpy as jnp
        import numpy as np
        N_NODES = 50000
        N_EDGES = 12500
        IN_DIM = 256
        OUT_DIM = 256
        HEADS = 1
        EDGE_DIM = 128
        NEG_SLOPE = 0.01
        key = jax.random.key(seed)
        ks = jax.random.split(key, 8)
        x = jax.random.normal(ks[0], (N_NODES, IN_DIM), dtype=jnp.float32)
        edge_index = jax.random.randint(ks[1], (2, N_EDGES), 0, N_NODES, dtype=jnp.int64)
        edge_attr = jax.random.normal(ks[2], (N_EDGES, EDGE_DIM), dtype=jnp.float32)
        hc = HEADS * OUT_DIM
        Wn = jax.random.normal(ks[3], (hc, IN_DIM), dtype=jnp.float32) / np.sqrt(IN_DIM)
        bn = jnp.zeros((hc,), dtype=jnp.float32)
        We = jax.random.normal(ks[4], (hc, EDGE_DIM), dtype=jnp.float32) / np.sqrt(EDGE_DIM)
        be = jnp.zeros((hc,), dtype=jnp.float32)
        attn = jax.random.normal(ks[5], (1, HEADS, OUT_DIM), dtype=jnp.float32) * np.sqrt(2.0 / (HEADS * OUT_DIM + 1))
        return {'x': x, 'edge_index': edge_index, 'edge_attr': edge_attr, 'Wn': Wn, 'bn': bn, 'We': We, 'be': be, 'attn': attn}
    _L0_gnn_all = _L0_gnn_setup()
    _L0_gnn_in = {k: v for k, v in _L0_gnn_all.items() if k in ('Wn', 'bn', 'We', 'be', 'attn')}
    del _L0_gnn_all

    def _L1_gnn_setup():
        import jax, jax.numpy as jnp
        import numpy as np
        N, E, D_IN, D_OUT = (50000, 25000, 256, 256)
        key = jax.random.key(seed)
        k1, k2, k3, k4, k5, k6 = jax.random.split(key, 6)
        x = jax.random.normal(k1, (N, D_IN), dtype=jnp.float32)
        edge_index = jax.random.randint(k2, (2, E), 0, N, dtype=jnp.int64)
        s = 1.0 / np.sqrt(D_IN)
        W1 = jax.random.uniform(k3, (D_OUT, D_IN), minval=-s, maxval=s, dtype=jnp.float32)
        b1 = jax.random.uniform(k4, (D_OUT,), minval=-s, maxval=s, dtype=jnp.float32)
        W2 = jax.random.uniform(k5, (D_OUT, D_IN), minval=-s, maxval=s, dtype=jnp.float32)
        b2 = jax.random.uniform(k6, (D_OUT,), minval=-s, maxval=s, dtype=jnp.float32)
        return {'x': x, 'W1': W1, 'b1': b1, 'W2': W2, 'b2': b2, 'edge_index': edge_index}
    _L1_gnn_all = _L1_gnn_setup()
    _L1_gnn_in = {k: v for k, v in _L1_gnn_all.items() if k in ('W1', 'b1', 'W2', 'b2')}
    del _L1_gnn_all
    return {'x': x, 'src': src, 'dst': dst, 'edge_attr_128': edge_attr_128, 'L0_gnn_Wn': _L0_gnn_in['Wn'], 'L0_gnn_bn': _L0_gnn_in['bn'], 'L0_gnn_We': _L0_gnn_in['We'], 'L0_gnn_be': _L0_gnn_in['be'], 'L0_gnn_attn': _L0_gnn_in['attn'], 'L1_gnn_W1': _L1_gnn_in['W1'], 'L1_gnn_b1': _L1_gnn_in['b1'], 'L1_gnn_W2': _L1_gnn_in['W2'], 'L1_gnn_b2': _L1_gnn_in['b2']}

def reference(x, src, dst, edge_attr_128, L0_gnn_Wn, L0_gnn_bn, L0_gnn_We, L0_gnn_be, L0_gnn_attn, L1_gnn_W1, L1_gnn_b1, L1_gnn_W2, L1_gnn_b2):
    import jax
    import jax.numpy as jnp

    def _L0_gnn_ref(x, edge_index, edge_attr, Wn, bn, We, be, attn):
        import jax, jax.numpy as jnp
        import numpy as np
        N_NODES = 50000
        N_EDGES = 12500
        IN_DIM = 256
        OUT_DIM = 256
        HEADS = 1
        EDGE_DIM = 128
        NEG_SLOPE = 0.01
        N = x.shape[0]
        H, C = (attn.shape[1], attn.shape[2])
        src, dst = (edge_index[0], edge_index[1])
        h = x @ Wn.T + bn
        e = edge_attr @ We.T + be
        xj = h[src].reshape(-1, H, C)
        ee = e.reshape(-1, H, C)
        a = jax.nn.leaky_relu(jnp.sum((xj + ee) * attn, axis=-1), NEG_SLOPE)
        m = jax.ops.segment_max(a, dst, num_segments=N)
        a = jnp.exp(a - m[dst])
        denom = jax.ops.segment_sum(a, dst, num_segments=N)
        a = a / (denom[dst] + 1e-16)
        msg = (xj * a[..., None]).reshape(-1, H * C)
        out = jax.ops.segment_sum(msg, dst, num_segments=N)
        return jax.nn.relu(out)

    def _L1_gnn_ref(x, W1, b1, W2, b2, edge_index):
        import jax, jax.numpy as jnp
        import numpy as np
        N, E, D_IN, D_OUT = (50000, 25000, 256, 256)
        dst = edge_index[0]
        nbr = edge_index[1]
        n = x.shape[0]
        agg = jax.ops.segment_sum(x[nbr], dst, num_segments=n)
        cnt = jax.ops.segment_sum(jnp.ones((nbr.shape[0],), x.dtype), dst, num_segments=n)
        mean = agg / jnp.maximum(cnt, 1.0)[:, None]
        return x @ W1.T + b1 + mean @ W2.T + b2
    edge_index = jnp.stack([src, dst])
    x = _layernorm(x + _L0_gnn_ref(x, edge_index, edge_attr_128, L0_gnn_Wn, L0_gnn_bn, L0_gnn_We, L0_gnn_be, L0_gnn_attn), axis=-1)
    x = _layernorm(x + _L1_gnn_ref(x, L1_gnn_W1, L1_gnn_b1, L1_gnn_W2, L1_gnn_b2, edge_index), axis=-1)
    return x

_drawn_inputs = setup_inputs


def setup_inputs(seed=0):
    import zlib

    import numpy as np

    out = dict(_drawn_inputs(seed))
    spreads = {'L0_gnn_bn': (0.0, 0.267), 'L0_gnn_be': (0.0, 2.0)}
    factors = {}
    for name, (base, spread) in spreads.items():
        noise = np.random.default_rng([zlib.crc32(name.encode()), seed]).standard_normal(out[name].shape)
        drawn = base * np.exp(spread * noise) if base else spread * noise
        out[name] = jnp.asarray(drawn.astype(out[name].dtype))
    for name, factor in factors.items():
        out[name] = (out[name] * factor).astype(out[name].dtype)
    return out
```

```python
from contextlib import ExitStack

import concourse.bass as bass
from concourse import mybir

P = 128
D = 256
DE = 128
GT = 4
LO = 256
XW = D + 1
BIG = 1.0e38
SKIP = 100000.0
EPS = 1e-5
SLOPE = 0.01
TINY = 1e-16

ALU = mybir.AluOpType
ACT = mybir.ActivationFunctionType
F32 = mybir.dt.float32
BF16 = mybir.dt.bfloat16
I32 = mybir.dt.int32
DST, SRC = 0, 1


def wait(eng, sem, value):
    if isinstance(value, int) and value <= 0:
        return
    eng.wait_ge(sem, value)


def steps(eng, n, unroll, head, tail, body):
    lo = -(-head // unroll)
    hi = (n - tail) // unroll
    for q in range(lo * unroll):
        body(q, q // unroll, q % unroll)
    with eng.Fori(lo, hi) as m:
        for u in range(unroll):
            body(m * unroll + u, m, u)
    for q in range(hi * unroll, n):
        body(q, q // unroll, q % unroll)


def build(nc, x, src, dst, edge_attr, Wn, bn, We, be, attn, W1, b1, W2, b2, out):
    N = x.shape[0]
    E = src.shape[0]
    T = -(-E // P)
    T = -(-T // GT) * GT
    Q = T // GT
    FT, LT = E // P, E % P
    GN = P * GT
    G = -(-N // GN)
    LP = (N - (G - 1) * GN) // GT
    assert (G - 1) * GN + LP * GT == N and N < 256 * 256 - 1
    PADKEY = float(N)
    HB = -(-(N // LO + 1) // 2)
    assert HB <= P
    EC = 2 * GT
    NEC = FT // EC

    x1_dram = nc.dram_tensor("x1_scratch", [N, D], F32).ap()
    keyrow_dram = [nc.dram_tensor(f"keys_scratch{k}", [T, P], F32).ap() for k in (DST, SRC)]
    order_dram = [nc.dram_tensor(f"order_scratch{k}", [T * P, 3], F32).ap() for k in (DST, SRC)]
    sorted_dram = [nc.dram_tensor(f"sorted_scratch{k}", [T, P], F32).ap() for k in (DST, SRC)]

    with ExitStack() as ctx:
        def sb(name, shape, dt=F32):
            return ctx.enter_context(nc.sbuf_tensor(name, shape, dt))

        def sem(name):
            return ctx.enter_context(nc.semaphore(name))

        def sems(name, n):
            return [sem(f"{name}{i}") for i in range(n)]

        bank = [ctx.enter_context(nc.psum_tensor(f"bank{i}", [P, 512], F32)) for i in range(8)]

        X = sb("X", [P, T, XW])
        flat16 = X[:].rearrange("p t c -> p (t c)").bitcast(BF16)
        onehot_lo = flat16[:, 0:T * LO].rearrange("p (t c) -> p t c", t=T)
        onehot_hi = flat16[:, T * LO:T * (LO + 2 * HB)].rearrange("p (t c) -> p t c", t=T)
        xin = [sb(f"xin{i}", [P, GT, D]) for i in range(4)]
        yout = [sb(f"yout{i}", [P, GT, D]) for i in range(4)]
        xT = [sb(f"xT{i}", [P, 2, 2, P]) for i in range(4)]
        wnT = sb("wnT", [P, 2, D])
        w1T = sb("w1T", [P, 2, D])
        w2T = sb("w2T", [P, 2, D])
        v_b = sb("v_b", [P, D])
        u_b = sb("u_b", [P, DE])
        c0 = sb("c0", [P, 1])
        ident = sb("ident", [P, P])
        ident16 = sb("ident16", [P, P], BF16)
        below = sb("below", [P, P])
        above = sb("above", [P, P])
        ones = sb("ones", [P, P])
        ones16 = sb("ones16", [3, P], BF16)
        zero16 = sb("zero16", [P, 512], BF16)
        downshift = sb("downshift", [P, P])
        firstlast = sb("firstlast", [P, P])
        lastrow = sb("lastrow", [P, P])
        iota_i = sb("iota_i", [P, LO], I32)
        iota_f = sb("iota_f", [P, LO])
        iota16 = sb("iota16", [P, LO], BF16)
        bias32 = yout[1][0:3]
        bias_rest = yout[2][0:3, 0:2]
        bias_up = yout[2][0:3, 2:4]
        bias_sel = yout[3][0:3, 0:2]
        bias16 = sb("bias16", [3, 2, D], BF16)
        attn_c = sb("attn_c", [P, 2])
        attn_b = sb("attn_b", [P, 2, P])
        bsum_c = sb("bsum_c", [P, 2, 2])
        bsum = sb("bsum", [P, 2])
        keyrow_i = [sb(f"keyrow_i{k}", [T, P], I32) for k in (DST, SRC)]
        keyrow_f = [sb(f"keyrow_f{k}", [T, P]) for k in (DST, SRC)]
        pay = sb("pay", [P, T, 3])
        key_i = sb("key_i", [P, T], I32)
        dig_i = sb("dig_i", [P, 2, T], I32)
        dig_f = [sb(f"dig_f{k}", [P, 2, T]) for k in (DST, SRC)]
        offs = sb("offs", [HB, 2])
        junk = sb("junk", [P, 2, D])
        earlier = sb("earlier", [P, T])
        found = sb("found", [P, T])
        rank_i = [sb(f"rank_i{k}", [P, T], I32) for k in (DST, SRC)]
        kB = [sb(f"kB{i}", [P, GT, P]) for i in range(2)]
        ordrow = sb("ordrow", [T, P, 3])
        krow = [sb(f"krow{k}", [T, P]) for k in (DST, SRC)]
        keyc = [sb(f"keyc{k}", [P, T + 1]) for k in (DST, SRC)]
        prevk = [sb(f"prevk{k}", [P, T + 1]) for k in (DST, SRC)]
        idx_tmp = sb("idx_tmp", [P, T])
        idx_src = [sb(f"idx_src{k}", [P, T], I32) for k in (DST, SRC)]
        idx_dst = [sb(f"idx_dst{k}", [P, T], I32) for k in (DST, SRC)]
        idx_out = [sb(f"idx_out{k}", [P, T], I32) for k in (DST, SRC)]
        pays = sb("pays", [P, 2, GT, 3])
        idxs = sb("idxs", [P, 3, 4, GT], I32)
        xdot = sb("xdot", [P, T])
        ealrow = sb("ealrow", [T, P])
        logit = sb("logit", [T, P])
        pen = sb("pen", [T, P + 1])
        fwd = sb("fwd", [T, P])
        bwd = sb("bwd", [T, P])
        tmp_r = sb("tmp_r", [T, P])
        carry = sb("carry", [1, 4, T])
        cpen = sb("cpen", [1, 2, T + 1])
        cscan = sb("cscan", [1, 4, T + 1])
        ccol = sb("ccol", [T, 4])
        wrow = sb("wrow", [T, P])
        weight = sb("weight", [P, T])
        sel = [sb(f"sel{i}", [P, GT, P]) for i in range(2)]
        csel = [sb(f"csel{i}", [P, GT, P]) for i in range(2)]
        agg = [sb(f"agg{i}", [P, GT, XW]) for i in range(2)]
        table = [t[0:HB].rearrange("p j c -> p (j c)").rearrange("p (b c) -> p b c", b=2) for t in sel]
        base, scanned = [t[0:HB].rearrange("p j c -> p (j c)").rearrange("p (b c) -> p b c", b=2) for t in csel]
        onehotT = [t[0:HB, 0, 0:2 * P].rearrange("p (b c) -> p b c", b=2) for t in agg]
        den = sb("den", [P, 2, GT])
        aggn = sb("aggn", [P, GT, D])
        stats = sb("stats", [P, 4, GT, 6])
        mv = sb("mv", [P, 4, GT, 2])
        std = sb("std", [P, 4, GT])
        rstd = sb("rstd", [P, 4, GT])
        nmr = sb("nmr", [P, 4, GT])
        eps_c = sb("eps_c", [P, 1])

        s_w = sem("weights_loaded")
        s_small = sem("small_inputs_loaded")
        s_krow = sem("key_rows_loaded")
        s_const = sem("pool_constants")
        s_chain = sem("dve_step")
        s_dconst = sem("dve_constants")
        s_wt = sem("weights_transposed")
        s_vu = sem("attn_products")
        s_keyf = sem("key_rows_float")
        s_keyt = sem("key_columns_psum")
        s_keyd = sem("key_rows_in_dram")
        s_ea = sems("edge_features_loaded", 4)
        s_eau = sem("edge_features_used")
        s_onehot = sems("onehots", 2)
        s_hist = sem("histogram")
        s_rowtot = sem("row_totals")
        s_offs = sem("row_offsets")
        s_base = sem("base_ready")
        s_seed = sem("table_seeded")
        s_kb = [sems(f"key_spread{k}_", 2) for k in (DST, SRC)]
        s_kbu = sems("key_spread_used", 2)
        s_hT = sems("onehot_turned", 2)
        s_hTc = sems("onehot_turned_copied", 2)
        s_tab = sems("table_copied", 2)
        s_add = sems("tile_counted", 2)
        s_look = sems("looked_up", 2)
        s_found = sems("found", 2)
        s_rank = sem("ranks")
        s_scat = [sems(f"order_scattered{k}_", 2) for k in (DST, SRC)]
        s_ord = sem("order_loaded")
        s_ordf = sem("order_rows_ready")
        s_ordt = sem("order_turned")
        s_keyc = sem("sorted_keys_ready")
        s_next = sem("next_keys")
        s_idx = sem("indices_ready")
        s_sortd = sem("sorted_keys_in_dram")
        s_xones = sem("ones_columns")
        s_xg = sem("src_rows_gathered")
        s_idxs = sems("index_columns_staged", 3)
        s_xin = sems("x_loaded", 4)
        s_st1 = sem("x_stats")
        s_sq1 = sem("x_std")
        s_x1 = sem("x1_ready")
        s_x1st = sems("x1_stored", 4)
        s_tp = sem("x1_turned")
        s_tpc = sem("x1_turned_copied")
        s_r = sem("r_ready")
        s_st2 = sem("r_stats")
        s_sq2 = sem("r_std")
        s_nm2 = sem("r_scales")
        s_y = sem("y_ready")
        s_yst = sems("y_stored", 4)
        s_xprod = sem("x_products")
        s_xdot = sem("x_dots")
        s_xdotT = sem("x_dots_turned")
        s_ends = sem("row_ends")
        s_endsT = sem("row_ends_turned")
        s_cs = sem("carries")
        s_csT = sem("carries_turned")
        s_expin = sem("exp_input")
        s_exp = sem("exp_done")
        s_wT = sem("weights_turned")
        s_wc = sem("edge_weights_ready")
        s_kb3 = [sems(f"sorted_spread{k}_", 2) for k in (DST, SRC)]
        s_sel = sems("select_ready", 2)
        s_agg = sems("aggregated", 2)
        s_raw = sems("aggregate_copied", 2)
        s_an = sems("aggregate_scaled", 2)
        s_tb = sems("aggregate_turned", 2)
        s_tbc = sems("aggregate_turned_copied", 2)
        s_h = sem("h_ready")
        s_hst = sem("h_added_to_x")
        s_hst2 = sem("h_stats")
        s_hsq = sem("h_std")
        s_ex1 = sem("edge_x1_ready")
        s_tc = sems("node_turned", 2)
        s_tcc = sems("node_turned_copied", 2)
        s_er = sems("edge_r_ready", 2)
        s_est = sems("edge_r_stats", 2)
        s_esq = sems("edge_r_std", 2)
        s_enm = sems("edge_r_scales", 2)
        s_ey = sems("edge_y_ready", 2)
        s_xd = sems("dst_x_rows_gathered", 2)
        s_xs = sems("src_x1_rows_gathered", 4)
        s_z = sems("neighbour_x1_rows_gathered", 4)
        s_x1sc = sems("x1_scattered", 2)
        s_ysc = [sems(f"y_scattered{k}_", 4) for k in (DST, SRC)]
        s_m = sems("moments", 4)
        s_rc = sems("reciprocals", 4)
        s_den = sems("denominators", 2)

        def wait_apart(eng, sem, value):
            if not isinstance(value, int):
                value = eng.to_reg(value)
                eng.wait_ge(s_const, 3)
            wait(eng, sem, value)

        def grp(dram, g, parts=P):
            if isinstance(g, int):
                return dram[g * GN:g * GN + parts * GT].rearrange("(p j) d -> p (j d)", j=GT)
            return dram[0:(G - 1) * GN].rearrange("(g p j) d -> p g (j d)", p=P, j=GT)[:, bass.ds(g, 1), :] \
                .rearrange("p a f -> p (a f)")

        def spread(dram, q):
            v = dram.rearrange("(q j) c -> q (j c)", j=GT)
            return v[bass.ds(q, 1), :].rearrange("a f -> (a f)").partition_broadcast(P)

        def counted(m, u, off, n):
            return m * (4 // n) + (u + off) // n

        def in_range(q, lo, hi):
            return not isinstance(q, int) or lo <= q < hi

        def parts(g):
            return LP if isinstance(g, int) and g == G - 1 else P

        def rbank(h_par, p):
            return bank[4 + 2 * h_par + p]

        def full(ap):
            return ap[:].rearrange("p j d -> p (j d)")

        block = ctx.enter_context(nc.Block())

        @block.sync
        def _(sp):
            for w, t in ((Wn, 0), (W1, 1), (W2, 2)):
                sp.dma_start(xin[t][:, 0:2, :], w.rearrange("(b p) k -> p b k", b=2)).then_inc(s_w, 16)
            sp.dma_start(yout[0][:, 0, :].rearrange("p (b k) -> p b k", b=2),
                         We.rearrange("(b p) k -> p b k", b=2)).then_inc(s_w, 16)
            sp.wait_ge(s_const, 1)
            for k, key in ((DST, dst), (SRC, src)):
                sp.dma_start(keyrow_i[k][0:FT, :], key[0:FT * P].rearrange("(t p) -> t p", p=P)).then_inc(s_krow, 16)
                sp.dma_start(keyrow_i[k][FT:FT + 1, 0:LT],
                             key[FT * P:E].rearrange("(a p) -> a p", a=1)).then_inc(s_krow, 16)
            with nc.allow_non_contiguous_dma(reason="256 weights of the attention vector and biases as columns"):
                sp.dma_start(attn_c[:], attn.rearrange("a h (b p) -> p (a h b)", b=2)).then_inc(s_small, 16)
                sp.dma_start(bsum_c[:, 0, :], bn.rearrange("(b p) -> p b", b=2)).then_inc(s_small, 16)
                sp.dma_start(bsum_c[:, 1, :], be.rearrange("(b p) -> p b", b=2)).then_inc(s_small, 16)
            for i, b in enumerate((bn, b1, b2)):
                sp.dma_start(bias32[:, i, :], b.partition_broadcast(3)).then_inc(s_small, 16)
            sp.wait_ge(s_wt, 3)
            sp.wait_ge(s_vu, 1)

            def features(c, m, u):
                wait_apart(sp, s_eau, EC * (c - 3))
                v = edge_attr[0:NEC * EC * P].rearrange("(c t p) d -> p c t d", p=P, t=EC)
                sp.dma_start(full(xin[u]).rearrange("p (t d) -> p t d", d=DE),
                             v[:, bass.ds(c, 1)].rearrange("p a t d -> p (a t) d")).then_inc(s_ea[u], 16)
            steps(sp, NEC, 4, 4, 0, features)
            c = NEC
            for t in range(NEC * EC, FT + 1):
                rows = P if t < FT else LT
                sp.wait_ge(s_eau, EC * (c - 3))
                sp.dma_start(xin[c % 4][0:rows, 0, 0:DE], edge_attr[t * P:t * P + rows]).then_inc(s_ea[c % 4], 16)
                c += 1

            for k in (DST, SRC):
                sp.wait_ge(s_keyd, 32)

                def load(q, m, u):
                    wait_apart(sp, s_kbu[k], q - 1)
                    if k == SRC and isinstance(q, int) and q < 2:
                        sp.wait_ge(s_kbu[DST], Q)
                    sp.dma_start(full(kB[u]), spread(keyrow_dram[k], q)).then_inc(s_kb[k][u], 16)
                steps(sp, Q, 2, 2, 0, load)

            sp.wait_ge(s_eau, FT + 1)

            def dense(g, m, u):
                last = isinstance(g, int) and g == G - 1
                if not isinstance(g, int) or g < G:
                    n = LP if last else P
                    wait_apart(sp, s_tp, 2 * (g - 4) + 2)
                    wait_apart(sp, s_x1st[u], 16 * m)
                    sp.dma_start(full(xin[u])[0:n], grp(x, g, n)).then_inc(s_xin[u], 16)
                if not isinstance(g, int) or 2 <= g < G + 2:
                    h, hu = g - 2, (u - 2) % 4
                    n = LP if isinstance(h, int) and h == G - 1 else P
                    wait_apart(sp, s_x1, GT * h + GT)
                    sp.dma_start(grp(x1_dram, h, n), full(xin[hu])[0:n]).then_inc(s_x1st[hu], 16)
                if not isinstance(g, int) or g >= 5:
                    h, hu = g - 5, (u - 5) % 4
                    n = LP if isinstance(h, int) and h == G - 1 else P
                    wait_apart(sp, s_y, GT * h + GT)
                    sp.dma_start(grp(out, h, n), full(yout[hu])[0:n]).then_inc(s_yst[hu], 16)
            steps(sp, G + 5, 4, 5, 7, dense)

            sp.wait_ge(s_sortd, 32)
            for k in (DST, SRC):

                def load3(q, m, u):
                    if k == SRC and isinstance(q, int) and q < 2:
                        sp.wait_ge(s_sel[DST], Q)
                    if k == DST and isinstance(q, int) and q < 2:
                        sp.wait_ge(s_kbu[SRC], Q)
                    wait_apart(sp, s_sel[k], q - 1)
                    sp.dma_start(full(kB[u]), spread(sorted_dram[k], q)).then_inc(s_kb3[k][u], 16)
                steps(sp, Q, 2, 2, 0, load3)

        @block.gpsimd
        def _(pool):
            g = nc.gpsimd
            for k in (DST, SRC):
                last = g.memset(keyrow_i[k][:], N)
            last.then_inc(s_const, 1)
            g.memset(ones[:], 1.0)
            g.memset(ones16[:], 1.0)
            g.memset(zero16[:], 0.0)
            g.memset(eps_c[:], EPS)
            g.iota(iota_i[:], pattern=[[1, LO]], base=0, channel_multiplier=0)
            for t in (ident, downshift, firstlast, lastrow, below):
                last = g.memset(t[:], 0.0)
            last = g.memset(above[:], 0.0)
            last.then_inc(s_const, 1)
            pool.wait_ge(s_const, 2)
            g.affine_select(out=ident[:], in_=ident[:], compare_op=ALU.not_equal, fill=1.0, base=0,
                            pattern=[[-1, P]], channel_multiplier=1)
            g.affine_select(out=downshift[:], in_=downshift[:], compare_op=ALU.not_equal, fill=1.0, base=-1,
                            pattern=[[-1, P]], channel_multiplier=1)
            g.affine_select(out=firstlast[:], in_=firstlast[:], compare_op=ALU.not_equal, fill=1.0, base=1 - P,
                            pattern=[[1, P]], channel_multiplier=P)
            g.affine_select(out=lastrow[:], in_=lastrow[:], compare_op=ALU.not_equal, fill=1.0, base=1 - P,
                            pattern=[[0, P]], channel_multiplier=1)
            g.affine_select(out=below[:], in_=below[:], compare_op=ALU.is_ge, fill=1.0, base=0,
                            pattern=[[1, P]], channel_multiplier=-1)
            g.affine_select(out=above[:], in_=above[:], compare_op=ALU.is_ge, fill=1.0, base=0,
                            pattern=[[-1, P]], channel_multiplier=1).then_inc(s_const, 1)

            staged = [0, 0, 0]

            def stage(role, idx, h, slot):
                g.tensor_copy(idxs[:, role, slot, :], idx[:, bass.ds(GT * h, GT)]).then_inc(s_idxs[role], 1)
                wait_apart(pool, s_idxs[role], staged[role] + h + 1)

            def at(role, slot, j):
                return bass.IndirectOffsetOnAxis(ap=idxs[:, role, slot, j:j + 1], axis=0)

            def gather(dst_ap, table, where, s):
                g.indirect_dma_start(out=dst_ap, out_offset=None, in_=table, in_offset=where).then_inc(s, 16)

            def scatter(table, src_ap, where, s):
                g.indirect_dma_start(out=table, out_offset=where, in_=src_ap, in_offset=None,
                                     bounds_check=N - 1, oob_is_err=False).then_inc(s, 16)

            def scatter_order(k):
                pool.wait_ge(s_rank, k + 1)
                for u in range(2 * k):
                    pool.wait_ge(s_scat[DST][u], 16 * GT * len(range(u, Q, 2)))

                def group(q, m, u):
                    wait_apart(pool, s_scat[k][u], 16 * GT * m)
                    g.tensor_copy(pays[:, u], pay[:, bass.ds(q * GT, GT), :])
                    stage(0, rank_i[k], q, u)
                    for j in range(GT):
                        g.indirect_dma_start(out=order_dram[k], out_offset=at(0, u, j), in_=pays[:, u, j, :],
                                             in_offset=None).then_inc(s_scat[k][u], 16)
                steps(pool, Q, 2, 2, 0, group)
                staged[0] += Q

            scatter_order(DST)
            pool.wait_ge(s_idx, 1)
            pool.wait_ge(s_xones, 1)

            for t in range(T):
                gather(X[:, t, 0:D], x, bass.IndirectOffsetOnAxis(ap=idx_src[DST][:, t:t + 1], axis=0), s_xg)
            scatter_order(SRC)

            pool.wait_ge(s_xg, 16 * T)
            for t in range(T):
                wait(pool, s_xdot, t - 1)
                nc.gpsimd.tensor_tensor(junk[:, t % 2, :], X[:, t, 0:D], v_b[:], ALU.mult).then_inc(s_xprod, 1)

            for u in range(2):
                pool.wait_ge(s_scat[SRC][u], 16 * GT * len(range(u, Q, 2)))

            for u in range(4):
                pool.wait_ge(s_x1st[u], 16 * len(range(u, G, 4)))
                pool.wait_ge(s_yst[u], 16 * len(range(u, G, 4)))

            def by_dst(q, m, u):
                known = isinstance(q, int)
                if not known or q < Q:
                    wait_apart(pool, s_hst, GT * (q - 1))
                    stage(0, idx_dst[DST], q, u % 2)
                    for j in range(GT):
                        gather(xin[u % 2][:, j, :], x, at(0, u % 2, j), s_xd[u % 2])
                if not known or 3 <= q < Q + 3:
                    h, hu = q - 3, (u - 3) % 4
                    wait_apart(pool, s_ey[DST], GT * h + GT)
                    stage(1, idx_out[DST], h, hu)
                    for j in range(GT):
                        scatter(out, yout[hu][:, j, :], at(1, hu, j), s_ysc[DST][hu])
                if not known or 2 <= q < Q + 2:
                    h, hu = q - 2, u % 2
                    wait_apart(pool, s_ex1, GT * h + GT)
                    stage(2, idx_out[DST], h, hu)
                    for j in range(GT):
                        scatter(x1_dram, xin[2 + hu][:, j, :], at(2, hu, j), s_x1sc[hu])
            steps(pool, Q + 3, 4, 4, 4, by_dst)
            staged = [n + Q for n in staged]

            for u in range(2):
                pool.wait_ge(s_x1sc[u], 16 * GT * len(range(u, Q, 2)))
            for u in range(4):
                pool.wait_ge(s_ysc[DST][u], 16 * GT * len(range(u, Q, 4)))

            def by_src(q, m, u):
                known = isinstance(q, int)
                if not known or q < Q:
                    wait_apart(pool, s_tc[SRC], 2 * (q - 3))
                    stage(0, idx_dst[SRC], q, u)
                    for j in range(GT):
                        gather(X[:, GT * u + j, 0:D], x1_dram, at(0, u, j), s_z[u])
                    stage(2, idx_src[SRC], q, u)
                    for j in range(GT):
                        gather(xin[u][:, j, :], x1_dram, at(2, u, j), s_xs[u])
                if not known or 3 <= q < Q + 3:
                    h, hu = q - 3, (u - 3) % 4
                    wait_apart(pool, s_ey[SRC], GT * h + GT)
                    stage(1, idx_out[SRC], h, hu)
                    for j in range(GT):
                        scatter(out, yout[hu][:, j, :], at(1, hu, j), s_ysc[SRC][hu])
            steps(pool, Q + 3, 4, 4, 4, by_src)
            for u in range(4):
                pool.wait_ge(s_ysc[SRC][u], 16 * GT * len(range(u, Q, 4)))


        @block.scalar
        def _(act):
            a = nc.scalar

            def turned_copy(dst_i, src_bank, ready, n_ready, users, copied):
                act.wait_ge(ready, n_ready)
                for s, n in users:
                    wait(act, s, n)
                a.copy(xT[dst_i][:].rearrange("p a b c -> p (a b c)"), src_bank[:, :]).then_inc(copied, 1)

            def root(slot, ready, n, done, rows=P):
                act.wait_ge(ready, n)
                a.activation(std[0:rows, slot, :], mv[0:rows, slot, :, 1], ACT.Sqrt, bias=eps_c[0:rows]).then_inc(done, 1)

            def y_rows(h_par, hu, slot, done, bank_of, rows=P, js=range(GT)):
                for j in js:
                    a.activation(yout[hu][0:rows, j, :], bank_of(j // 2)[0:rows, (j % 2) * D:(j % 2 + 1) * D],
                                 ACT.Identity, bias=nmr[0:rows, slot, j:j + 1],
                                 scale=rstd[0:rows, slot, j:j + 1]).then_inc(done, 1)

            for k in (DST, SRC):
                act.wait_ge(s_keyf, k + 1)
                act.dma_start(keyrow_dram[k], keyrow_f[k][:]).then_inc(s_keyd, 16)

            for k in (DST, SRC):
                act.wait_ge(s_seed, k + 1)

                def table_copy(q, m, u):
                    for j in range(GT):
                        t = q * GT + j
                        wait(act, s_add[k], t)
                        wait(act, s_look[k], t - 1)
                        a.copy(table[j % 2].rearrange("p b c -> p (b c)"), bank[2][0:HB, :]).then_inc(s_tab[k], 1)
                steps(act, Q, 4, 1, 0, table_copy)

            def load_order(k):
                for u in range(2):
                    act.wait_ge(s_scat[k][u], 16 * GT * len(range(u, Q, 2)))
                act.dma_start(ordrow[:], order_dram[k].rearrange("(t p) c -> t p c", p=P)).then_inc(s_ord, 16)

            def store_sorted(k):
                act.wait_ge(s_ordf, k + 1)
                act.dma_start(sorted_dram[k], krow[k][:]).then_inc(s_sortd, 16)

            load_order(DST)
            store_sorted(DST)
            act.wait_ge(s_vu, 1)

            def dense_copy(h, h_par, p):
                turned_copy(2 * h_par + p, bank[p], s_tp, 2 * h + p + 1, [(s_r, 2 * (h - 2) + p + 1)], s_tpc)

            root(0, s_st1, 1, s_sq1)
            root(1, s_st1, 2, s_sq1)
            root(0, s_st1, 3, s_sq1)
            for h in range(2):
                for p in range(2):
                    dense_copy(h, h, p)

            def x_dot(t, par):
                act.wait_ge(s_xprod, t + 1)
                a.activation(junk[:, par, :], junk[:, par, :], ACT.Copy,
                             accum_out=xdot[:, bass.ds(t, 1)]).then_inc(s_xdot, 1)

            def dense(g, m, u, t=None):
                if t is not None:
                    x_dot(t, 0)
                root(2 + u % 2, s_st2, g + 1, s_sq2, parts(g))
                if t is not None:
                    x_dot(t + 1, 1)
                if in_range(g, 0, G - 3):
                    root((u + 1) % 2, s_st1, g + 4, s_sq1, parts(g + 3) if isinstance(g, int) else P)
                act.wait_ge(s_nm2, g + 1)
                wait(act, s_yst[u], 16 * m)
                for p in range(2):
                    if in_range(g, 0, G - 2):
                        dense_copy(g + 2, u % 2, p)
                    y_rows(u % 2, u, 2 + u % 2, s_y, lambda b: rbank(u % 2, b), parts(g), (2 * p, 2 * p + 1))

            half = -(-(G - T // 2) // 4) * 4
            for g in range(4):
                dense(g, 0, g)
            with act.Fori(1, half // 4) as m:
                for u in range(4):
                    dense(m * 4 + u, m, u)
            with act.Fori(half // 4, (G - 6) // 4) as m:
                for u in range(4):
                    dense(m * 4 + u, m, u, m * 8 + (2 * u - 2 * half))
            for g in range((G - 6) // 4 * 4, G):
                dense(g, g // 4, g % 4, 2 * (g - half))
            for t in range(2 * (G - half), T):
                x_dot(t, t % 2)

            act.wait_ge(s_idx, 1)
            load_order(SRC)

            act.wait_ge(s_expin, 1)
            a.activation(wrow[:], logit[:], ACT.Exp).then_inc(s_exp, 1)
            store_sorted(SRC)

            def raw(k, q, u, j):
                act.wait_ge(s_agg[k], q * GT + j + 1)
                wait(act, s_an[k], q - 1)
                a.copy(agg[u % 2][:, j, :], bank[2 + j % 2][:, 0:XW]).then_inc(s_raw[k], 1)

            for u in range(4):
                act.wait_ge(s_yst[u], 16 * len(range(u, G, 4)))

            def by_dst(q, m, u):
                def cp_agg(p):
                    if in_range(q, 1, Q + 1):
                        h = q - 1
                        turned_copy(p, bank[p], s_tb[DST], 2 * h + p + 1, [(s_h, 2 * (h - 1) + p + 1)], s_tbc[DST])

                def cp_node(p):
                    if in_range(q, 2, Q + 2):
                        h = q - 2
                        turned_copy(2 + p, bank[p], s_tc[DST], 2 * h + p + 1, [(s_er[DST], 2 * (h - 1) + p + 1)],
                                    s_tcc[DST])
                for j in range(GT):
                    if in_range(q, 0, Q):
                        raw(DST, q, u, j)
                    (cp_agg if j < 2 else cp_node)(j % 2)
                    if j == 1 and in_range(q, 3, Q + 3):
                        root(2 + (u - 3) % 2, s_est[DST], q - 2, s_esq[DST])
                if in_range(q, 3, Q + 3):
                    hu = (u - 3) % 4
                    act.wait_ge(s_enm[DST], q - 2)
                    wait(act, s_ysc[DST][hu], 16 * GT * counted(m, u, -3, 4))
                    y_rows(0, hu, 2 + (u - 3) % 2, s_ey[DST], lambda p: bank[6 + p])
                if in_range(q, 1, Q + 1):
                    root((u - 1) % 2, s_hst2, q, s_hsq)
            steps(act, Q + 3, 4, 8, 4, by_dst)

            for u in range(4):
                act.wait_ge(s_ysc[DST][u], 16 * GT * len(range(u, Q, 4)))

            def by_src(q, m, u):
                def cp(p, node):
                    if in_range(q, 1, Q + 1):
                        h = q - 1
                        ready, done = (s_tc, s_tcc) if node else (s_tb, s_tbc)
                        turned_copy(2 * node + p, bank[node], ready[SRC], 2 * h + p + 1,
                                    [(s_er[SRC], 2 * (h - 1) + p + 1)], done[SRC])
                for j in range(GT):
                    if in_range(q, 0, Q):
                        raw(SRC, q, u, j)
                    cp(j // 2, j % 2)
                    if j == 1 and in_range(q, 2, Q + 2):
                        root(2 + u % 2, s_est[SRC], q - 1, s_esq[SRC])
                if in_range(q, 2, Q + 2):
                    hu = (u - 2) % 4
                    act.wait_ge(s_enm[SRC], q - 1)
                    wait(act, s_ysc[SRC][hu], 16 * GT * counted(m, u, -2, 4))
                    y_rows(0, hu, 2 + u % 2, s_ey[SRC], lambda p: rbank(u % 2, p))
            steps(act, Q + 2, 4, 8, 3, by_src)

        @block.vector
        def _(dve):
            v = nc.vector
            done = [0]

            def then(ins):
                done[0] += 1
                ins.then_inc(s_chain, 1)
                dve.wait_ge(s_chain, done[0])

            def ts(o, i, s1, s2, o0, o1=None):
                return v.tensor_scalar(o, i, s1, s2, o0, o1) if o1 is not None else v.tensor_scalar(o, i, s1, s2, o0)

            def stt(o, i0, s, i1, o0, o1, **kw):
                return v.scalar_tensor_tensor(out=o, in0=i0, scalar=s, in1=i1, op0=o0, op1=o1, **kw)

            dve.wait_ge(s_const, 3)
            dve.wait_ge(s_small, 96)
            for b in range(2):
                v.tensor_scalar(attn_b[:, b, :], ones[:], attn_c[:, b:b + 1], None, ALU.mult)
            v.tensor_tensor(bsum[:], bsum_c[:, 0, :], bsum_c[:, 1, :], ALU.add).then_inc(s_dconst, 1)

            then(v.tensor_tensor(bias32[:, 1, :], bias32[:, 1, :], bias32[:, 2, :], ALU.add))
            then(v.tensor_copy(bias_rest, bias32[:, 0:2, :]))
            for i in range(3):
                then(v.tensor_copy(bias16[:], bias_rest))
                then(v.tensor_copy(bias_up, bias16[:]))
                if i == 0:
                    then(ts(bias_sel, bias_up, ident[0:3, 0:1], None, ALU.mult))
                else:
                    for b in range(2):
                        then(stt(bias_sel[:, b, :], bias_up[:, b, :], ident[0:3, i:i + 1], bias_sel[:, b, :],
                                 ALU.mult, ALU.add))
                then(v.tensor_tensor(bias_rest, bias_rest, bias_up, ALU.subtract))
            v.tensor_copy(bias16[:], bias_sel).then_inc(s_dconst, 1)

            then(v.tensor_copy(iota_f[:], iota_i[:]))
            v.tensor_copy(iota16[:], iota_i[:])
            v.tensor_copy(ident16[:], ident[:]).then_inc(s_dconst, 1)
            dve.wait_ge(s_krow, 64)
            for k in (DST, SRC):
                v.tensor_copy(keyrow_f[k][:], keyrow_i[k][:]).then_inc(s_keyf, 1)

            dve.wait_ge(s_wt, 3)
            for w, t in enumerate((wnT, w1T, w2T)):
                then(v.tensor_copy(t[:].rearrange("p b c -> p (b c)"), bank[w][:, :]))
            for b in range(2):
                then(v.tensor_tensor(w1T[:, b, b * P:(b + 1) * P], w1T[:, b, b * P:(b + 1) * P], ident[:], ALU.add))
            dve.wait_ge(s_vu, 1)
            v.tensor_copy(v_b[:], bank[3][:, 0:D])
            v.tensor_copy(u_b[:], bank[4][:, 0:DE])
            then(v.tensor_copy(c0[:], bank[5][:, 0:1]))

            for k in (DST, SRC):
                dve.wait_ge(s_keyt, k + 1)
                v.tensor_copy(pay[:, :, k], bank[6 + k][:, 0:T])
                then(v.tensor_copy(key_i[:], bank[6 + k][:, 0:T]))
                v.tensor_single_scalar(dig_i[:, 0, :], key_i[:], LO - 1, ALU.bitwise_and)
                then(v.tensor_single_scalar(dig_i[:, 1, :], key_i[:], LO.bit_length() - 1, ALU.arith_shift_right))
                ins = v.tensor_copy(dig_f[k][:], dig_i[:])
                if k == SRC:
                    ins.then_inc(s_dconst, 1)

            then(v.memset(pay[:, FT:T, 2], 0.0))

            def feature_dot(buf, i, t, rows=P):
                f = full(buf)[0:rows, i * DE:(i + 1) * DE]
                stt(f, f, 1.0, u_b[0:rows], ALU.mult, ALU.mult,
                    accum_out=pay[0:rows, bass.ds(t, 1), 2]).then_inc(s_eau, 1)

            def features(c, m, u):
                dve.wait_ge(s_ea[u], 16 * (m + 1))
                for i in range(EC):
                    feature_dot(xin[u], i, c * EC + i)
            steps(dve, NEC, 4, 0, 0, features)
            for c, t in enumerate(range(NEC * EC, FT + 1), start=NEC):
                dve.wait_ge(s_ea[c % 4], 16 * (c // 4 + 1))
                feature_dot(xin[c % 4], 0, t, P if t < FT else LT)

            def sort(k):
                if k == SRC:
                    dve.wait_ge(s_add[DST], T)

                def onehots(q, m, u):
                    for j in range(GT):
                        t = q * GT + j
                        ts(onehot_lo[:, bass.ds(t, 1), :].rearrange("p a c -> p (a c)"), iota16[:],
                           dig_f[k][:, 0, bass.ds(t, 1)], None, ALU.is_equal)
                        ins = ts(onehot_hi[:, bass.ds(t, 1), :].rearrange("p a c -> p (a c)"), iota16[:, 0:2 * HB],
                                 dig_f[k][:, 1, bass.ds(t, 1)], None, ALU.is_equal)
                    ins.then_inc(s_onehot[k], 1)
                steps(dve, Q, 4, 0, 0, onehots)
                dve.wait_ge(s_hist, k + 1)
                for b in range(2):
                    ins = v.tensor_tensor_scan(scanned[:, b, :], zero16[0:HB, 0:LO], bank[0][0:HB, b * LO:(b + 1) * LO],
                                               0.0, ALU.add, ALU.add)
                ins.then_inc(s_rowtot, 1)
                dve.wait_ge(s_offs, k + 1)
                then(v.tensor_copy(offs[:], bank[1][0:HB, 0:2]))
                for b in range(2):
                    ins = stt(base[:, b, :], scanned[:, b, :], offs[:, b:b + 1], bank[0][0:HB, b * LO:(b + 1) * LO],
                              ALU.add, ALU.subtract)
                ins.then_inc(s_base, 1)

                def lookup(t, par):
                    dve.wait_ge(s_look[k], t + 1)
                    stt(bank[5 + par][:, 0:LO], iota_f[:], dig_f[k][:, 0, bass.ds(t, 1)], bank[5 + par][:, 0:LO],
                        ALU.is_equal, ALU.mult, accum_out=found[:, bass.ds(t, 1)]).then_inc(s_found[k], 1)

                def tiles(q, m, u):
                    for j in range(GT):
                        t = q * GT + j
                        dve.wait_ge(s_hT[k], t + 1)
                        wait(dve, s_look[k], t - 1)
                        v.tensor_copy(onehotT[j % 2], bank[3 + j % 2][0:HB, 0:P].bitcast(BF16)
                                      .rearrange("p (b c) -> p b c", b=2)).then_inc(s_hTc[k], 1)
                        if j == 0:
                            dve.wait_ge(s_kb[k][u % 2], 16 * (counted(m, u, 0, 2) + 1))
                        ins = stt(kB[u % 2][:, j, :], kB[u % 2][:, j, :], pay[:, bass.ds(t, 1), k], below[:],
                                  ALU.is_equal, ALU.mult, accum_out=earlier[:, bass.ds(t, 1)])
                        if j == GT - 1:
                            ins.then_inc(s_kbu[k], 1)
                        if not (isinstance(t, int) and t == 0):
                            lookup(t - 1, (j - 1) % 2)
                steps(dve, Q, 4, 2, 0, tiles)
                lookup(T - 1, (T - 1) % 2)
                dve.wait_ge(s_found[k], T)
                v.tensor_tensor(rank_i[k][:], earlier[:], found[:], ALU.add).then_inc(s_rank, 1)

            def ordered(k):
                own, other = (idx_dst, idx_src) if k == DST else (idx_src, idx_dst)
                dve.wait_ge(s_ord, 16 * (k + 1))
                v.tensor_copy(krow[k][:], ordrow[:, :, k])
                if k == DST:
                    v.tensor_copy(ealrow[:], ordrow[:, :, 2])
                v.tensor_copy(tmp_r[:], ordrow[:, :, 1 - k]).then_inc(s_ordf, 1)
                dve.wait_ge(s_ordt, k + 1)
                v.memset(keyc[k][:, T:T + 1], PADKEY + 1)
                v.memset(prevk[k][:, 0:1], -1.0)
                ts(own[k][:], bank[0][:, 0:T], N - 1.0, None, ALU.min)
                ts(other[k][:], bank[1][:, 0:T], N - 1.0, None, ALU.min)
                v.tensor_copy(keyc[k][:, 0:T], bank[0][:, 0:T]).then_inc(s_keyc, 1)
                dve.wait_ge(s_next, k + 1)
                v.tensor_copy(prevk[k][:, 1:T + 1], bank[3][:, 0:T])
                then(v.tensor_tensor(idx_tmp[:], keyc[k][:, 0:T], bank[2][:, 0:T], ALU.is_equal))
                stt(idx_out[k][:], idx_tmp[:], SKIP, keyc[k][:, 0:T], ALU.mult, ALU.add).then_inc(s_idx, 1)

            dve.wait_ge(s_dconst, 4)
            sort(DST)
            sort(SRC)
            dve.wait_ge(s_add[SRC], T)
            v.memset(X[:, :, D:XW].rearrange("p t c -> p (t c)"), 1.0).then_inc(s_xones, 1)
            ordered(DST)

            def moments(slot, src_of, rows, h):
                for j in range(GT):
                    ins = v.bn_stats(stats[0:rows, slot, j, :], src_of(j))
                ins.then_inc(s_m[slot], 1)
                wait_apart(dve, s_m[slot], h)
                for j in range(GT):
                    ins = v.bn_aggr(mv[0:rows, slot, j, :], stats[0:rows, slot, j, :])
                return ins

            n_m = [0] * 4

            def invert(slot, rows, h):
                v.reciprocal(rstd[0:rows, slot, :], std[0:rows, slot, :]).then_inc(s_rc[slot], 1)
                dve.wait_ge(s_rc[slot], h)

            def scales(slot, rows):
                return stt(nmr[0:rows, slot, :], mv[0:rows, slot, :, 0], -1.0, rstd[0:rows, slot, :], ALU.mult, ALU.mult)

            def normalise(buf, slot, rows, ready):
                for j in range(GT):
                    ts(buf[0:rows, j, :], buf[0:rows, j, :], mv[0:rows, slot, j, 0:1], rstd[0:rows, slot, j:j + 1],
                       ALU.subtract, ALU.mult).then_inc(ready, 1)

            def stats_x(g, m, u, off, js):
                n = parts(g)
                if js[0] == 0:
                    dve.wait_ge(s_xin[(u + off) % 4], 16 * (counted(m, u, off, 4) + 1))
                for j in js:
                    ins = v.bn_stats(stats[0:n, (u + off) % 2, j, :], xin[(u + off) % 4][0:n, j, :])
                if js[-1] == GT - 1:
                    ins.then_inc(s_m[(u + off) % 2], 1)

            def moments_of(slot, rows, h, done):
                wait_apart(dve, s_m[slot], h)
                for j in range(GT):
                    ins = v.bn_aggr(mv[0:rows, slot, j, :], stats[0:rows, slot, j, :])
                ins.then_inc(done, 1)

            def invert_x(g, m, u, off):
                dve.wait_ge(s_sq1, g + 1)
                slot, n = (u + off) % 2, parts(g)
                v.reciprocal(rstd[0:n, slot, :], std[0:n, slot, :]).then_inc(s_rc[slot], 1)

            def norm_x(g, m, u, off):
                dve.wait_ge(s_rc[(u + off) % 2], counted(m, u, off, 2) + 1)
                normalise(xin[(u + off) % 4], (u + off) % 2, parts(g), s_x1)

            for h in range(3):
                if h == 2:
                    dve.wait_ge(s_x1, GT)
                stats_x(h, 0, 0, h, range(GT))
                moments_of(h % 2, P, h // 2 + 1, s_st1)
                if h < 2:
                    invert_x(h, 0, 0, h)
                    norm_x(h, 0, 0, h)

            def dense(g, m, u):
                n, slot = parts(g), 2 + u % 2
                turns = counted(m, u, 0, 2) + 1
                more2, more3 = in_range(g, 0, G - 2), in_range(g, 0, G - 3)
                for j in range(GT):
                    if j % 2 == 0:
                        dve.wait_ge(s_r, 2 * g + j // 2 + 1)
                    ins = v.bn_stats(stats[0:n, slot, j, :],
                                     rbank(u % 2, j // 2)[0:n, (j % 2) * D:(j % 2 + 1) * D])
                    if j == 0 and more2:
                        invert_x(g + 2, m, u, 2)
                    if j == 1 and more2:
                        norm_x(g + 2, m, u, 2)
                ins.then_inc(s_m[slot], 1)
                if more3:
                    stats_x(g + 3, m, u, 3, (0, 1))
                moments_of(slot, n, turns, s_st2)
                if more3:
                    stats_x(g + 3, m, u, 3, (2, 3))
                dve.wait_ge(s_sq2, g + 1)
                v.reciprocal(rstd[0:n, slot, :], std[0:n, slot, :]).then_inc(s_rc[slot], 1)
                if more3:
                    moments_of((u + 3) % 2, parts(g + 3), counted(m, u, 3, 2) + 1, s_st1)
                dve.wait_ge(s_rc[slot], turns)
                scales(slot, n).then_inc(s_nm2, 1)
            steps(dve, G, 4, 4, 6, dense)
            n_m = [G // 2 + (i % 2 < G % 2) for i in range(4)]


            dve.wait_ge(s_xdotT, 1)
            then(stt(logit[:], bank[0][0:T, 0:P], c0[0:T], ealrow[:], ALU.add, ALU.add))
            then(stt(logit[:], logit[:], SLOPE, logit[:], ALU.mult, ALU.max))
            v.memset(pen[:, 0:1], 0.0)
            v.memset(pen[:, P:P + 1], 0.0)
            kr = krow[DST]
            then(v.tensor_tensor(pen[:, 1:P], kr[:, 1:P], kr[:, 0:P - 1], ALU.is_equal))
            then(ts(pen[:, 1:P], pen[:, 1:P], 1.0, BIG, ALU.subtract, ALU.mult))
            v.tensor_tensor_scan(fwd[:], pen[:, 0:P], logit[:], -BIG, ALU.add, ALU.max)
            then(v.tensor_tensor_scan(bwd[:, ::-1], pen[:, 1:P + 1][:, ::-1], logit[:, ::-1], -BIG, ALU.add, ALU.max))
            v.tensor_copy(tmp_r[:, 0:1], fwd[:, P - 1:P]).then_inc(s_ends, 1)
            dve.wait_ge(s_endsT, 1)
            then(v.tensor_copy(carry[:], bank[1][0:1, :].rearrange("p (i c) -> p i c", i=4)[:, :, 0:T]))
            v.memset(cpen[:], 0.0)
            then(v.memset(cscan[:, 0:2, :], -BIG))
            then(v.memset(cscan[:, 2:4, :], -1.0))
            v.tensor_copy(cscan[:, 2, 1:T + 1], carry[:, 2, :])
            v.tensor_copy(cscan[:, 3, 0:T], carry[:, 3, :])
            v.tensor_tensor(cpen[:, 0, 1:T], carry[:, 2, 1:T], carry[:, 2, 0:T - 1], ALU.is_equal)
            then(v.tensor_tensor(cpen[:, 1, 1:T], carry[:, 3, 1:T], carry[:, 3, 0:T - 1], ALU.is_equal))
            then(ts(cpen[:, :, 1:T], cpen[:, :, 1:T], 1.0, BIG, ALU.subtract, ALU.mult))
            v.tensor_tensor_scan(cscan[:, 0, 1:T + 1], cpen[:, 0, 0:T], carry[:, 0, :], -BIG, ALU.add, ALU.max)
            v.tensor_tensor_scan(cscan[:, 1, 0:T][:, ::-1], cpen[:, 1, 1:T + 1][:, ::-1], carry[:, 1, :][:, ::-1],
                                 -BIG, ALU.add, ALU.max).then_inc(s_cs, 1)
            dve.wait_ge(s_csT, 1)
            then(v.tensor_copy(ccol[:], bank[2][0:T, 0:4]))
            for i, part in enumerate((fwd, bwd)):
                then(ts(tmp_r[:], kr[:], ccol[:, 2 + i:3 + i], None, ALU.is_equal))
                then(ts(tmp_r[:], tmp_r[:], 1.0, BIG, ALU.subtract, ALU.mult))
                then(stt(part[:], tmp_r[:], ccol[:, i:i + 1], part[:], ALU.add, ALU.max))
            then(v.tensor_tensor(fwd[:], fwd[:], bwd[:], ALU.max))
            v.tensor_tensor(logit[:], logit[:], fwd[:], ALU.subtract).then_inc(s_expin, 1)
            dve.wait_ge(s_wT, 1)
            v.tensor_copy(weight[:], bank[3][:, 0:T]).then_inc(s_wc, 1)
            dve.wait_ge(s_wc, 1)
            ordered(SRC)

            def select(k, q, m, u, off):
                par = (u + off) % 2
                dve.wait_ge(s_kb3[k][par], 16 * (counted(m, u, off, 2) + 1))
                wait(dve, s_agg[k], GT * (q - 1))
                for j in range(GT):
                    t = q * GT + j
                    if k == DST:
                        ts(sel[par][:, j, :], kB[par][:, j, :], keyc[k][:, bass.ds(t, 1)], weight[:, bass.ds(t, 1)],
                           ALU.is_equal, ALU.mult)
                    else:
                        ts(sel[par][:, j, :], kB[par][:, j, :], keyc[k][:, bass.ds(t, 1)], None, ALU.is_equal)
                    ins = ts(csel[par][:, j, :], kB[par][:, j, :], prevk[k][:, bass.ds(t, 1)], lastrow[:, 0:1],
                             ALU.is_equal, ALU.mult)
                ins.then_inc(s_sel[k], 1)

            def scale(k, q, u):
                s = agg[u % 2]
                dve.wait_ge(s_raw[k], GT * q + GT)
                wait(dve, s_tb[k], 2 * q)
                col = s[:, :, D:XW].rearrange("p j c -> p (j c)")
                ts(den[:, 0, :], col, TINY if k == DST else 1.0, None,
                   ALU.add if k == DST else ALU.max).then_inc(s_den[k], 1)
                dve.wait_ge(s_den[k], 2 * q + 1)
                v.reciprocal(den[:, 1, :], den[:, 0, :]).then_inc(s_den[k], 1)
                dve.wait_ge(s_den[k], 2 * q + 2)
                for j in range(GT):
                    ins = ts(aggn[:, j, :], s[:, j, 0:D], den[:, 1, j:j + 1], None, ALU.mult)
                ins.then_inc(s_an[k], 1)

            def y_stats(k, h, m, u, off, bank_of):
                slot = 2 + (u + off) % 2
                dve.wait_ge(s_er[k], 2 * h + 2)
                moments(slot, lambda j: bank_of(j // 2)[:, (j % 2) * D:(j % 2 + 1) * D], P,
                        n_m[slot] + counted(m, u, off, 2) + 1).then_inc(s_est[k], 1)
                dve.wait_ge(s_esq[k], h + 1)
                invert(slot, P, n_m[slot] + counted(m, u, off, 2) + 1)
                scales(slot, P).then_inc(s_enm[k], 1)

            dve.wait_ge(s_kb3[DST][0], 16)
            select(DST, 0, 0, 0, 0)

            def by_dst(q, m, u):
                if in_range(q, 0, Q - 1):
                    select(DST, q + 1, m, u, 1)
                if in_range(q, 3, Q + 3):
                    y_stats(DST, q - 3, m, u, -3, lambda p: bank[6 + p])
                if in_range(q, 1, Q + 1):
                    h, par = q - 1, (u - 1) % 2
                    x1 = xin[2 + par]
                    dve.wait_ge(s_xd[par], 16 * GT * (counted(m, u, -1, 2) + 1))
                    wait(dve, s_x1sc[par], 16 * GT * counted(m, u, -1, 2))
                    wait(dve, s_tc[DST], 2 * (h - 1))
                    for j in range(GT):
                        if j % 2 == 0:
                            dve.wait_ge(s_h, 2 * h + j // 2 + 1)
                        stt(x1[:, j, :], bank[4 + j // 2][:, (j % 2) * D:(j % 2 + 1) * D], 0.0, xin[par][:, j, :],
                            ALU.max, ALU.add).then_inc(s_hst, 1)
                    dve.wait_ge(s_hst, GT * h + GT)
                    moments(par, lambda j: x1[:, j, :], P, n_m[par] + counted(m, u, -1, 2) + 1).then_inc(s_hst2, 1)
                if in_range(q, 0, Q):
                    scale(DST, q, u)
                if in_range(q, 1, Q + 1):
                    dve.wait_ge(s_hsq, q)
                    invert(par, P, n_m[par] + counted(m, u, -1, 2) + 1)
                    normalise(x1, par, P, s_ex1)
            steps(dve, Q + 3, 4, 4, 4, by_dst)
            n_m = [n + Q // 2 + (i % 2 < Q % 2) for i, n in enumerate(n_m)]

            dve.wait_ge(s_kb3[SRC][0], 16)
            select(SRC, 0, 0, 0, 0)

            def by_src(q, m, u):
                if in_range(q, 0, Q - 1):
                    select(SRC, q + 1, m, u, 1)
                if in_range(q, 2, Q + 2):
                    y_stats(SRC, q - 2, m, u, -2, lambda p: rbank(u % 2, p))
                if in_range(q, 0, Q):
                    scale(SRC, q, u)
            steps(dve, Q + 2, 4, 4, 3, by_src)

        @block.tensor
        def _(pe):
            mm = nc.tensor.matmul
            tr = nc.tensor.transpose

            pe.wait_ge(s_const, 3)
            pe.wait_ge(s_w, 64)
            for w in range(3):
                for b in range(2):
                    for kb in range(2):
                        ins = tr(bank[w][:, kb * D + b * P:kb * D + (b + 1) * P],
                                 xin[w][:, b, kb * P:(kb + 1) * P], ident[:])
                ins.then_inc(s_wt, 1)
            pe.wait_ge(s_dconst, 1)
            for b in range(2):
                mm(bank[3][:, 0:D], attn_b[:, b, :], xin[0][:, b, :], start=b == 0, stop=b == 1)
            for b in range(2):
                mm(bank[4][:, 0:DE], attn_b[:, b, :], yout[0][:, 0, b * DE:(b + 1) * DE], start=b == 0, stop=b == 1)
            for b in range(2):
                ins = mm(bank[5][:, 0:1], attn_b[:, b, :], bsum[:, b:b + 1], start=b == 0, stop=b == 1)
            ins.then_inc(s_vu, 1)
            for k in (DST, SRC):
                pe.wait_ge(s_keyf, k + 1)
                tr(bank[6 + k][:, 0:T], keyrow_f[k][:], ident[0:T, 0:T]).then_inc(s_keyt, 1)
            pe.wait_ge(s_dconst, 4)

            def zeros(o, **kw):
                return mm(o, zero16[:, 0:HB], zero16[:], skip_group_check=True, **kw)

            def count_tile(o, t):
                for b in range(2):
                    ins = mm(o[:, b * LO:(b + 1) * LO],
                             onehot_hi[:, bass.ds(t, 1), b * HB:(b + 1) * HB].rearrange("p a c -> p (a c)"),
                             onehot_lo[:, bass.ds(t, 1), :].rearrange("p a c -> p (a c)"),
                             start=False, stop=False, skip_group_check=True)
                return ins

            def sort(k):
                zeros(bank[0][0:HB, :], start=True, stop=False)

                def count(q, m, u):
                    pe.wait_ge(s_onehot[k], q + 1)
                    for j in range(GT):
                        count_tile(bank[0][0:HB, :], q * GT + j)
                steps(pe, Q, 4, 0, 0, count)
                zeros(bank[0][0:HB, :], start=False, stop=True).then_inc(s_hist, 1)
                pe.wait_ge(s_rowtot, k + 1)
                tot = scanned[:, :, LO - 1:LO].rearrange("p b c -> p (b c)")
                mm(bank[1][0:HB, 0:2], above[0:HB, 0:HB], tot, start=True, stop=False, skip_group_check=True)
                mm(bank[1][0:HB, 1:2], ones[0:HB, 0:HB], tot[:, 0:1], start=False, stop=True,
                   skip_group_check=True).then_inc(s_offs, 1)
                pe.wait_ge(s_base, k + 1)
                mm(bank[2][0:HB, :], ident[0:HB, 0:HB], base.rearrange("p b c -> p (b c)"), start=True, stop=False,
                   skip_group_check=True).then_inc(s_seed, 1)

                def turn(t, par):
                    wait(pe, s_hTc[k], t - 1)
                    o = bank[3 + par][0:HB, 0:P].bitcast(BF16)
                    for b in range(2):
                        ins = tr(o[:, b * P:(b + 1) * P],
                                 onehot_hi[:, bass.ds(t, 1), b * HB:(b + 1) * HB].rearrange("p a c -> p (a c)"),
                                 ident16[:])
                    ins.then_inc(s_hT[k], 1)

                def tiles(q, m, u):
                    for j in range(GT):
                        t = q * GT + j
                        if not isinstance(t, int) or t + 1 < T:
                            turn(t + 1, (j + 1) % 2)
                        pe.wait_ge(s_tab[k], t + 1)
                        count_tile(bank[2][0:HB, :], t).then_inc(s_add[k], 1)
                        pe.wait_ge(s_hTc[k], t + 1)
                        wait(pe, s_found[k], t - 1)
                        for b in range(2):
                            ins = mm(bank[5 + j % 2][:, 0:LO], onehotT[j % 2][:, b, :], table[j % 2][:, b, :],
                                     start=b == 0, stop=b == 1)
                        ins.then_inc(s_look[k], 1)
                turn(0, 0)
                steps(pe, Q, 4, 1, 1, tiles)
                zeros(bank[2][0:HB, :], start=False, stop=True)

            def ordered(k):
                pe.wait_ge(s_ordf, k + 1)
                tr(bank[0][:, 0:T], krow[k][:], ident[0:T, 0:T])
                tr(bank[1][:, 0:T], tmp_r[:], ident[0:T, 0:T]).then_inc(s_ordt, 1)
                pe.wait_ge(s_keyc, k + 1)
                mm(bank[2][:, 0:T], downshift[:], keyc[k][:, 0:T], start=True, stop=False)
                mm(bank[2][:, 0:T], firstlast[:], keyc[k][:, 1:T + 1], start=False, stop=True)
                mm(bank[3][:, 0:T], lastrow[:], keyc[k][:, 0:T], start=True, stop=True).then_inc(s_next, 1)

            sort(DST)
            sort(SRC)
            ordered(DST)
            pe.wait_ge(s_idx, 1)
            pe.wait_ge(s_found[SRC], T)

            def turn_pair(o, buf, p, n=P):
                for jj in range(2):
                    for c in range(2):
                        at = (2 * jj + c) * P
                        ins = tr(o[:, at:at + n], buf[0:n, 2 * p + jj, c * P:(c + 1) * P], ident[0:n, 0:n])
                return ins

            def products(o, terms, bias, n=P):
                for jj in range(2):
                    to = o[0:n, jj * D:(jj + 1) * D]
                    mm(to, ones16[:, 0:n], bias16[:, bias, :], start=True, stop=False)
                    for i, (buf, w) in enumerate(terms):
                        for c in range(2):
                            ins = mm(to, buf[:, jj, c, 0:n], w[:, c, :], start=False,
                                     stop=i == len(terms) - 1 and c == 1)
                return ins

            def turn(h, hu, p):
                pe.wait_ge(s_x1, GT * h + 2 * p + 2)
                wait(pe, s_tpc, 2 * (h - 1) + p + 1)
                turn_pair(bank[p], xin[hu], p, parts(h)).then_inc(s_tp, 1)

            def product(h, par, p):
                pe.wait_ge(s_tpc, 2 * h + p + 1)
                wait(pe, s_y, GT * (h - 2) + 2 * p + 2)
                products(rbank(par, p), [(xT[2 * par + p], w1T)], 1, parts(h)).then_inc(s_r, 1)

            turn(0, 0, 0)
            turn(0, 0, 1)

            def dense(g, m, u):
                product(g, u % 2, 0)
                if in_range(g, 0, G - 1):
                    turn(g + 1, (u + 1) % 4, 0)
                    turn(g + 1, (u + 1) % 4, 1)
                product(g, u % 2, 1)
            steps(pe, G, 4, 4, 6, dense)

            pe.wait_ge(s_xdot, T)
            pe.wait_ge(s_tpc, 2 * G)
            tr(bank[0][0:T, 0:P], xdot[:], ident[:]).then_inc(s_xdotT, 1)
            pe.wait_ge(s_ends, 1)
            for i, col in enumerate((fwd[:, P - 1:P], bwd[:, 0:1], krow[DST][:, P - 1:P], krow[DST][:, 0:1])):
                ins = tr(bank[1][0:1, i * P:i * P + T], col, ident[0:T, 0:T])
            ins.then_inc(s_endsT, 1)
            pe.wait_ge(s_cs, 1)
            for i, lo in enumerate((0, 1, 0, 1)):
                ins = tr(bank[2][0:T, i:i + 1], cscan[0:1, i, lo:lo + T], ident[0:1, 0:1])
            ins.then_inc(s_csT, 1)
            pe.wait_ge(s_exp, 1)
            tr(bank[3][:, 0:T], wrow[:], ident[0:T, 0:T]).then_inc(s_wT, 1)
            ordered(SRC)
            pe.wait_ge(s_idx, 2)

            def aggregate(k, q, m, u, j):
                t = q * GT + j
                first = isinstance(t, int) and t == 0
                o = bank[2 + j % 2][:, 0:XW]
                pe.wait_ge(s_sel[k], q + 1)
                if k == SRC and j == 0:
                    pe.wait_ge(s_z[u], 16 * GT * (m + 1))
                wait(pe, s_raw[k], t - 1)
                rows = X[:, bass.ds(t, 1), :].rearrange("p a c -> p (a c)") if k == DST else X[:, GT * u + j, :]
                ins = mm(o, sel[u % 2][:, j, :], rows, start=True, stop=first)
                if not first:
                    wait(pe, s_raw[k], t)
                    before = agg[u % 2][:, j - 1, :] if j else agg[(u - 1) % 2][:, GT - 1, :]
                    ins = mm(o, csel[u % 2][:, j, :], before, start=False, stop=True)
                ins.then_inc(s_agg[k], 1)

            def turn_sums(k, h, p, b, users):
                pe.wait_ge(s_an[k], h + 1)
                for s, n in users:
                    wait(pe, s, n)
                turn_pair(bank[b], aggn, p).then_inc(s_tb[k], 1)

            pe.wait_ge(s_xg, 16 * T)
            pe.wait_ge(s_wc, 1)
            pe.wait_ge(s_y, GT * G)

            def by_dst(q, m, u):
                def agg_(j):
                    if in_range(q, 0, Q):
                        aggregate(DST, q, m, u, j)

                def turn_b(p):
                    if in_range(q, 1, Q + 1):
                        turn_sums(DST, q - 1, p, p, [(s_tcc[DST], 2 * (q - 3) + p + 1)])

                def turn_c(p):
                    if in_range(q, 2, Q + 2):
                        h = q - 2
                        pe.wait_ge(s_ex1, GT * h + 2 * p + 2)
                        if in_range(q, 1, Q + 1):
                            pe.wait_ge(s_tbc[DST], 2 * (q - 1) + p + 1)
                        else:
                            pe.wait_ge(s_tcc[DST], 2 * (h - 1) + p + 1)
                        turn_pair(bank[p], xin[2 + u % 2], p).then_inc(s_tc[DST], 1)

                def prod_b(p):
                    if in_range(q, 1, Q + 1):
                        h = q - 1
                        pe.wait_ge(s_tbc[DST], 2 * h + p + 1)
                        wait(pe, s_hst, GT * (h - 1) + 2 * p + 2)
                        products(bank[4 + p], [(xT[p], wnT)], 0).then_inc(s_h, 1)

                def prod_c(p):
                    if in_range(q, 2, Q + 2):
                        h = q - 2
                        pe.wait_ge(s_tcc[DST], 2 * h + p + 1)
                        wait(pe, s_ey[DST], GT * (h - 1) + 2 * p + 2)
                        products(bank[6 + p], [(xT[2 + p], w1T)], 1).then_inc(s_er[DST], 1)
                agg_(0)
                turn_b(0)
                agg_(1)
                turn_b(1)
                agg_(2)
                prod_b(0)
                turn_c(0)
                agg_(3)
                turn_c(1)
                prod_b(1)
                prod_c(0)
                prod_c(1)
            steps(pe, Q + 3, 4, 4, 4, by_dst)

            pe.wait_ge(s_tcc[DST], 2 * Q)
            pe.wait_ge(s_ey[DST], GT * Q)

            def by_src(q, m, u):
                def turn_x(p):
                    if in_range(q, 1, Q + 1):
                        h = q - 1
                        pe.wait_ge(s_xs[(u - 1) % 4], 16 * GT * (counted(m, u, -1, 4) + 1))
                        wait(pe, s_tcc[SRC], 2 * h + p)
                        turn_pair(bank[1], xin[(u - 1) % 4], p).then_inc(s_tc[SRC], 1)

                def turn_b(p):
                    if in_range(q, 1, Q + 1):
                        turn_sums(SRC, q - 1, p, 0, [(s_tbc[SRC], 2 * (q - 1) + p)])
                for j in range(GT):
                    if in_range(q, 0, Q):
                        aggregate(SRC, q, m, u, j)
                    (turn_x if j % 2 else turn_b)(j // 2)
                if in_range(q, 1, Q + 1):
                    h = q - 1
                    for p in range(2):
                        pe.wait_ge(s_tbc[SRC], 2 * h + p + 1)
                        pe.wait_ge(s_tcc[SRC], 2 * h + p + 1)
                        wait(pe, s_ey[SRC], GT * (h - 2) + 2 * p + 2)
                        products(rbank((u - 1) % 2, p), [(xT[p], w2T), (xT[2 + p], w1T)], 1).then_inc(s_er[SRC], 1)
            steps(pe, Q + 2, 4, 4, 3, by_src)


INPUTS = ["x", "src", "dst", "edge_attr_128", "L0_gnn_Wn", "L0_gnn_bn", "L0_gnn_We", "L0_gnn_be", "L0_gnn_attn",
          "L1_gnn_W1", "L1_gnn_b1", "L1_gnn_W2", "L1_gnn_b2"]


def kernel(**inputs):
    import numpy as np
    import concourse.bacc as bacc
    from concourse.bass_utils import run_bass_kernel_spmd

    nc = bacc.Bacc("TRN2", target_bir_lowering=False, num_devices=1)
    arrays, args = {}, []
    for name in INPUTS:
        a = np.ascontiguousarray(inputs[name])
        arrays[f"in_{name}"] = a
        args.append(nc.dram_tensor(f"in_{name}", a.shape, mybir.dt.from_np(a.dtype), kind="ExternalInput").ap())
    out = nc.dram_tensor("out_rows", inputs["x"].shape, F32, kind="ExternalOutput").ap()
    build(nc, *args, out)
    r = run_bass_kernel_spmd(nc, [arrays], core_ids=[0])
    return r.results[0]["out_rows"]
```
